# Optimizing a Trainium2 kernel written in Bass

```python
import numpy as np
import jax
import jax.numpy as jnp

def _softmax(x, axis=-1):
    return jax.nn.softmax(x, axis=axis)

def _gelu(x):
    return jax.nn.gelu(x, approximate=True)

def _silu(x):
    return jax.nn.silu(x)

def _sigmoid(x):
    return jax.nn.sigmoid(x)

def _layernorm(x, axis=-1, eps=1e-05):
    m = jnp.mean(x, axis=axis, keepdims=True)
    v = jnp.var(x, axis=axis, keepdims=True)
    return (x - m) / jnp.sqrt(v + eps)

def _scatter_add(tgt, idx, src, axis=0):
    return tgt.at[idx].add(src)

def _segment_sum(src, seg, n):
    return jax.ops.segment_sum(src, seg, n)
kernel_name = 'mk_adaln_ffn_d1_seqx_r8_17c719'

def setup_inputs(seed: int=0):
    np.random.seed(seed)
    _w = jnp.asarray

    def _rec_inputs():
        import jax
        import jax.numpy as jnp
        _rk = jax.random.key(seed)
        x = -0.000125 + 0.9999 * jax.random.normal(jax.random.fold_in(_rk, 1), (32, 32, 512), jnp.float32)
        _lenS = 32 - jax.random.randint(jax.random.fold_in(_rk, 7), (32,), 0, max(1, 32 // 4) + 1, jnp.int32)
        _lenS2 = 32 - jax.random.randint(jax.random.fold_in(_rk, 8), (32,), 0, max(1, 32 // 4) + 1, jnp.int32)
        itok_B_0_7 = jax.random.randint(jax.random.fold_in(_rk, 11), (32,), 0, 8, jnp.int32)
        return (x, itok_B_0_7)
    x, itok_B_0_7 = _rec_inputs()

    def _L0_cond_setup():
        import jax, jax.numpy as jnp
        import numpy as np
        TOP_K = 2
        LANG_BIAS = 5.0
        SCALING = 32.0 / 16.0
        LANGUAGE_PAD_ID = -1
        key = jax.random.key(seed)
        ks = jax.random.split(key, 6)
        B, T, D, O, E, R = (4, 256, 512, 512, 8, 16)
        x = jax.random.normal(ks[0], (B, T, D), dtype=jnp.float32)
        language_ids = jax.random.randint(ks[1], (B,), 0, E).astype(jnp.int64)
        W = jax.random.normal(ks[2], (O, D), dtype=jnp.float32) * (1.0 / np.sqrt(D))
        Wr = jax.random.normal(ks[3], (E, D), dtype=jnp.float32) * (1.0 / np.sqrt(D))
        A = jax.random.normal(ks[4], (E, R, D), dtype=jnp.float32) * (1.0 / np.sqrt(D))
        Bm = jax.random.normal(ks[5], (O, R), dtype=jnp.float32) * 0.0
        Bm = jnp.broadcast_to(Bm, (E, O, R)) + jax.random.normal(ks[5], (E, O, R), dtype=jnp.float32) * 0.02
        return {'x': x, 'language_ids': language_ids, 'W': W, 'Wr': Wr, 'A': A, 'B': Bm}
    _L0_cond_all = _L0_cond_setup()
    _L0_cond_in = {k: v for k, v in _L0_cond_all.items() if k in ('W', 'Wr', 'A', 'B')}
    del _L0_cond_all

    def _L0_ffn_setup():
        import jax, jax.numpy as jnp
        import numpy as np
        C_CLAMP = 0.5
        EPS = 1e-06
        key = jax.random.key(seed)
        ks = jax.random.split(key, 6)
        B_, S, D, O, R, E = (4, 256, 512, 512, 16, 8)
        x = jax.random.normal(ks[0], (B_, S, D), dtype=jnp.float32)
        W = jax.random.normal(ks[1], (O, D), dtype=jnp.float32) * (1.0 / np.sqrt(D))
        b = jax.random.normal(ks[2], (O,), dtype=jnp.float32) * 0.01
        A = jax.random.normal(ks[3], (E, D, R), dtype=jnp.float32) * (1.0 / np.sqrt(D))
        Bm = jax.random.normal(ks[4], (E, R, O), dtype=jnp.float32) * (1.0 / np.sqrt(R))
        p_scores = jax.random.uniform(ks[5], (E,), dtype=jnp.float32)
        return {'x': x, 'W': W, 'b': b, 'A': A, 'B': Bm, 'p_scores': p_scores}
    _L0_ffn_all = _L0_ffn_setup()
    _L0_ffn_in = {k: v for k, v in _L0_ffn_all.items() if k in ('W', 'b', 'A', 'B', 'p_scores')}
    del _L0_ffn_all
    return {'x': x, 'itok_B_0_7': itok_B_0_7, 'L0_cond_W': _L0_cond_in['W'], 'L0_cond_Wr': _L0_cond_in['Wr'], 'L0_cond_A': _L0_cond_in['A'], 'L0_cond_B': _L0_cond_in['B'], 'L0_ffn_W': _L0_ffn_in['W'], 'L0_ffn_b': _L0_ffn_in['b'], 'L0_ffn_A': _L0_ffn_in['A'], 'L0_ffn_B': _L0_ffn_in['B'], 'L0_ffn_p_scores': _L0_ffn_in['p_scores']}

def reference(x, itok_B_0_7, L0_cond_W, L0_cond_Wr, L0_cond_A, L0_cond_B, L0_ffn_W, L0_ffn_b, L0_ffn_A, L0_ffn_B, L0_ffn_p_scores):
    import jax
    import jax.numpy as jnp

    def _L0_cond_ref(x, language_ids, W, Wr, A, B):
        import jax, jax.numpy as jnp
        import numpy as np
        TOP_K = 2
        LANG_BIAS = 5.0
        SCALING = 32.0 / 16.0
        LANGUAGE_PAD_ID = -1
        base = jnp.einsum('btd,od->bto', x, W)
        E = Wr.shape[0]
        logits = jnp.einsum('btd,ed->bte', x.astype(jnp.float32), Wr.astype(jnp.float32))
        expert_targets = language_ids
        valid = expert_targets >= 0
        tgt = jnp.where(valid, expert_targets, 0)
        bias = jax.nn.one_hot(tgt, E, dtype=logits.dtype) * LANG_BIAS
        bias = jnp.where(valid[:, None], bias, 0.0)
        logits = logits + bias[:, None, :]
        topw, topi = jax.lax.top_k(logits, TOP_K)
        weights = jax.nn.softmax(topw, axis=-1)
        gates = jnp.sum(jax.nn.one_hot(topi, E, dtype=weights.dtype) * weights[..., None], axis=-2)
        gates = gates.astype(x.dtype)
        h = jnp.einsum('btd,erd->bter', x, A)
        lora_out = jnp.einsum('bter,bte,eor->bto', h, gates, B)
        return base + SCALING * lora_out

    def _L0_ffn_ref(x, W, b, A, B, p_scores):
        import jax, jax.numpy as jnp
        import numpy as np
        C_CLAMP = 0.5
        EPS = 1e-06
        z = jnp.einsum('bsd,od->bso', x, W) + b
        u = jnp.einsum('bsd,edr->ebsr', x, A)
        m = jnp.einsum('ebsr,ero,e->bso', u, B, p_scores)
        norm_z = jnp.linalg.norm(z, axis=-1, keepdims=True)
        norm_m = jnp.linalg.norm(m, axis=-1, keepdims=True)
        gamma = jnp.minimum(C_CLAMP * norm_z / (norm_m + EPS), 1.0)
        return z + gamma * m
    x = x + _L0_ffn_ref(_L0_cond_ref(x, itok_B_0_7, L0_cond_W, L0_cond_Wr, L0_cond_A, L0_cond_B), L0_ffn_W, L0_ffn_b, L0_ffn_A, L0_ffn_B, L0_ffn_p_scores)
    return x

_drawn_inputs = setup_inputs


def setup_inputs(seed=0):
    import zlib

    import numpy as np

    out = dict(_drawn_inputs(seed))
    spreads = {}
    factors = {'L0_cond_Wr': 5.04, 'L0_ffn_b': 8.0}
    for name, (base, spread) in spreads.items():
        noise = np.random.default_rng([zlib.crc32(name.encode()), seed]).standard_normal(out[name].shape)
        drawn = base * np.exp(spread * noise) if base else spread * noise
        out[name] = jnp.asarray(drawn.astype(out[name].dtype))
    for name, factor in factors.items():
        out[name] = (out[name] * factor).astype(out[name].dtype)
    return out
```

```python
from contextlib import ExitStack

import concourse.bass as bass
import concourse.mybir as mybir

ALU = mybir.AluOpType
ACT = mybir.ActivationFunctionType
AX_X = mybir.AxisListType.X
F32 = mybir.dt.float32
F32R = mybir.dt.float32r
I32 = mybir.dt.int32
U32 = mybir.dt.uint32

P = 128
LANG_BIAS = 5.0
SCALING = 32.0 / 16.0
C_CLAMP = 0.5
EPS = 1e-6


def lora_ffn_kernel(nc: bass.Bass, x_tok, x_feat, w_fold, a_route, ffn_B, ffn_b, p_rows, lang, out):
    T, D = x_tok.shape
    O = ffn_B.shape[1]
    ER = ffn_B.shape[0]
    E = a_route.shape[2] - ER
    R = ER // E
    KC = D // P
    FC = KC + 1
    W = D + ER
    NT = T // P
    HT = NT // 2
    HALF = HT * P
    HL = ER + E
    assert D == O == HALF == 512 and ER == P and FC * P == W

    GROUPS = [(0, 1, 2), (3, 4, 5), (6, 7)]
    GROUP_BANK = [7, 0, 1]
    Z_BANKS = (2, 3, 4)
    M_BANKS = (5, 6)
    GT_BANK = (7, 0)
    U_BANK = (6, 1)
    U_FOLD_BANKS = (5, 6)

    SPLITS = [("fold", 0), ("fold", 1), ("route", 0), ("x", 0), ("fold", 2), ("fold", 3), ("x", 1), ("B", 0)]

    def split_no(*key):
        return SPLITS.index(key) + 1

    with ExitStack() as ctx:
        def sb(name, shape, dt):
            return ctx.enter_context(nc.sbuf_tensor(name, shape, dt))

        def sem(name):
            return ctx.enter_context(nc.semaphore(name))

        fold_f = sb("fold_f", [P, KC, 2 * W], F32)
        route_f = sb("route_f", [P, KC, HL], F32)
        x_f = sb("x_f", [P, 2, KC, HALF], F32)
        B_f = sb("B_f", [P, O], F32)
        x_out = sb("x_out", [P, NT, D], F32)
        bias_b = sb("bias_b", [P, O], F32)
        p_col = sb("p_col", [P, 1], F32)
        lang_i = sb("lang_i", [P, NT], I32)

        fold_hi = sb("fold_hi", [P, KC, 2 * W], F32R)
        fold_lo = sb("fold_lo", [P, KC, 2 * W], F32R)
        route_hi = sb("route_hi", [P, KC, HL], F32R)
        route_lo = sb("route_lo", [P, KC, HL], F32R)
        x_hi = sb("x_hi", [P, 2, KC, HALF], F32R)
        x_lo = sb("x_lo", [P, 2, KC, HALF], F32R)
        pB_f = sb("pB_f", [P, O], F32)
        B_hi = sb("B_hi", [P, O], F32R)
        B_lo = sb("B_lo", [P, O], F32R)
        mz_hi = sb("mz_hi", [P, FC, O], F32R)
        mz_lo = sb("mz_lo", [P, FC, O], F32R)
        mu_hi = sb("mu_hi", [P, FC, ER], F32R)
        mu_lo = sb("mu_lo", [P, FC, ER], F32R)
        gt_hi = sb("gt_hi", [P, 2, HALF], F32R)
        gt_lo = sb("gt_lo", [P, 2, HALF], F32R)
        u_hi = sb("u_hi", [P, 2, HALF], F32R)
        u_lo = sb("u_lo", [P, 2, HALF], F32R)

        ident = sb("ident", [P, P], F32)
        experts = sb("experts", [P, E], F32)
        lang_bias = sb("lang_bias", [P, NT, E], F32)
        logits = sb("logits", [P, NT, E], F32)
        top8 = sb("top8", [P, NT, 8], F32)
        top8_at = sb("top8_at", [P, NT, 8], U32)
        top_at = sb("top_at", [P, NT, 2], F32)
        margin = sb("margin", [P, NT], F32)
        e_margin = sb("e_margin", [P, NT], F32)
        half_den = sb("half_den", [P, NT], F32)
        weight = sb("weight", [P, NT, 2], F32)
        chosen = sb("chosen", [P, NT, 2, E], F32)
        chosen_w = sb("chosen_w", [P, NT, 2, E], F32)
        gates = sb("gates", [P, NT, E], F32)
        gated = sb("gated", [P, NT, ER], F32)

        z_b = sb("z_b", [P, 3, O], F32)
        square = sb("square", [P, 2, O], F32)
        norm2 = sb("norm2", [P, NT, 2], F32)
        norm = sb("norm", [P, NT, 2], F32)
        m_den = sb("m_den", [P, NT], F32)
        m_inv = sb("m_inv", [P, NT], F32)
        gamma = sb("gamma", [P, NT], F32)

        bank = [ctx.enter_context(nc.psum_tensor(f"bank{i}", [P, 512], F32)) for i in range(8)]

        fold_in = [sem(f"fold_in{k}") for k in range(KC)]
        route_in = sem("route_in")
        x_in = [sem(f"x_in{h}") for h in range(2)]
        xt_in = [sem(f"xt_in{h}") for h in range(2)]
        B_in = sem("B_in")
        bias_in = sem("bias_in")
        p_in = sem("p_in")
        lang_in = sem("lang_in")
        hi_done = sem("hi_done")
        lo_done = sem("lo_done")
        pB_done = sem("pB_done")
        zeroed = sem("zeroed")
        ident_done = sem("ident_done")
        experts_done = sem("experts_done")
        lang_f_done = sem("lang_f_done")
        fold_z = sem("fold_z")
        fold_u = sem("fold_u")
        mz_hi_done = sem("mz_hi_done")
        mz_lo_done = sem("mz_lo_done")
        mu_hi_done = sem("mu_hi_done")
        mu_lo_done = sem("mu_lo_done")
        hl_done = sem("hl_done")
        gate_step = sem("gate_step")
        margin_done = sem("margin_done")
        exp_done = sem("exp_done")
        gated_done = sem("gated_done")
        gt_done = sem("gt_done")
        gt_hi_done = sem("gt_hi_done")
        gt_lo_done = sem("gt_lo_done")
        u_done = sem("u_done")
        u_hi_done = sem("u_hi_done")
        u_lo_done = sem("u_lo_done")
        z_done = sem("z_done")
        m_done = sem("m_done")
        zb_done = sem("zb_done")
        z_squared = sem("z_squared")
        m_squared = sem("m_squared")
        norm_done = sem("norm_done")
        gamma_step = sem("gamma_step")
        xz_done = sem("xz_done")
        out_done = sem("out_done")
        stored = sem("stored")

        def hl_at(t):
            g = next(g for g, tiles in enumerate(GROUPS) if t in tiles)
            c = GROUPS[g].index(t) * HL
            return bank[GROUP_BANK[g]][:, c:c + HL]

        block = ctx.enter_context(nc.Block())

        @block.sync
        def _(sp):
            sp.dma_start(fold_f[:, 0, :], w_fold[0]).then_inc(fold_in[0], 16)
            sp.dma_start(fold_f[:, 1, :], w_fold[1]).then_inc(fold_in[1], 16)
            sp.dma_start(route_f[:], a_route).then_inc(route_in, 16)
            sp.dma_start(x_f[:, 0], x_feat[0]).then_inc(x_in[0], 16)
            sp.dma_start(fold_f[:, 2, :], w_fold[2]).then_inc(fold_in[2], 16)
            sp.dma_start(fold_f[:, 3, :], w_fold[3]).then_inc(fold_in[3], 16)
            sp.dma_start(x_f[:, 1], x_feat[1]).then_inc(x_in[1], 16)
            sp.dma_start(B_f[:], ffn_B).then_inc(B_in, 16)
            sp.dma_start(bias_b[:], ffn_b.partition_broadcast(P)).then_inc(bias_in, 16)
            x_rows = x_tok.rearrange("(t p) d -> p t d", p=P)
            for h in range(2):
                tiles = slice(h * HT, (h + 1) * HT)
                sp.dma_start(x_out[:, tiles, :], x_rows[:, tiles, :]).then_inc(xt_in[h], 16)
            for t in range(NT):
                sp.wait_ge(out_done, t + 1)
                sp.dma_start(out[t * P:(t + 1) * P, :], x_out[:, t, :]).then_inc(stored, 16)
            sp.wait_ge(stored, 16 * NT)

        @block.gpsimd
        def _(pool):
            pool.dma_start(lang_i[:], lang).then_inc(lang_in, 16)
            pool.dma_start(p_col[:], p_rows).then_inc(p_in, 16)
            pool.memset(ident[:], 0.0).then_inc(zeroed, 1)
            pool.iota(experts[:], pattern=[[1, E]], base=0, channel_multiplier=0,
                      allow_small_or_imprecise_dtypes=True).then_inc(experts_done, 1)
            pool.wait_ge(zeroed, 1)
            pool.affine_select(out=ident[:], in_=ident[:], compare_op=ALU.not_equal, fill=1.0, base=0,
                               pattern=[[-1, P]], channel_multiplier=1).then_inc(ident_done, 1)
            for t in range(NT):
                if t % HT == 0:
                    pool.wait_ge(xt_in[t // HT], 16)
                pool.wait_ge(zb_done, t + 1)
                pool.tensor_tensor(x_out[:, t, :], x_out[:, t, :], z_b[:, t % 3, :], ALU.add).then_inc(xz_done, 1)

        @block.scalar
        def _(act):
            def split_hi(key, raw, hi, landed):
                act.wait_ge(landed, 16)
                act.activation(hi, raw, ACT.Copy).then_inc(hi_done, 1)

            def exp_margin(g):
                act.wait_ge(margin_done, g + 1)
                t0, t1 = GROUPS[g][0], GROUPS[g][-1] + 1
                act.activation(e_margin[:, t0:t1], margin[:, t0:t1], ACT.Exp).then_inc(exp_done, 1)

            def fold_z_hi(b):
                act.wait_ge(fold_z, b + 1)
                act.activation(mz_hi[:, b, :], bank[b][:], ACT.Copy).then_inc(mz_hi_done, 1)

            def fold_u_hi(n):
                act.wait_ge(fold_u, n + 1)
                dst = mu_hi[:, 0:KC, :] if n == 0 else mu_hi[:, KC, :]
                src = bank[U_FOLD_BANKS[0]][:].rearrange("p (b c) -> p b c", b=KC) if n == 0 else \
                    bank[U_FOLD_BANKS[1]][:, 0:ER]
                act.activation(dst, src, ACT.Copy).then_inc(mu_hi_done, 1)

            def gated_hi(h):
                act.wait_ge(gt_done, h + 1)
                act.activation(gt_hi[:, h, :], bank[GT_BANK[h]][:], ACT.Copy).then_inc(gt_hi_done, 1)

            def u_high(h):
                act.wait_ge(u_done, h + 1)
                act.activation(u_hi[:, h, :], bank[U_BANK[h]][:], ACT.Copy).then_inc(u_hi_done, 1)

            def square_z(t):
                act.wait_ge(zb_done, t + 1)
                if t >= 1:
                    act.wait_ge(z_squared, t)
                act.activation(square[:, 0, :], z_b[:, t % 3, :], ACT.Square,
                               accum_out=norm2[:, t, 0:1]).then_inc(z_squared, 1)

            def square_m(t):
                act.wait_ge(m_done, t + 1)
                if t >= 1:
                    act.wait_ge(m_squared, t)
                act.activation(square[:, 1, :], bank[M_BANKS[t % 2]][:], ACT.Square,
                               accum_out=norm2[:, t, 1:2]).then_inc(m_squared, 1)
                act.wait_ge(z_squared, t + 1)
                act.wait_ge(m_squared, t + 1)
                act.activation(norm[:, t, :], norm2[:, t, :], ACT.Sqrt).then_inc(norm_done, 1)

            split_hi("fold 0", fold_f[:, 0, :], fold_hi[:, 0, :], fold_in[0])
            split_hi("fold 1", fold_f[:, 1, :], fold_hi[:, 1, :], fold_in[1])
            split_hi("route", route_f[:], route_hi[:], route_in)
            split_hi("x 0", x_f[:, 0], x_hi[:, 0], x_in[0])
            split_hi("fold 2", fold_f[:, 2, :], fold_hi[:, 2, :], fold_in[2])
            split_hi("fold 3", fold_f[:, 3, :], fold_hi[:, 3, :], fold_in[3])
            exp_margin(0)
            split_hi("x 1", x_f[:, 1], x_hi[:, 1], x_in[1])
            act.wait_ge(p_in, 16)
            act.wait_ge(B_in, 16)
            act.activation(pB_f[:], B_f[:], ACT.Copy, scale=p_col[:, 0:1]).then_inc(pB_done, 1)
            act.wait_ge(pB_done, 1)
            act.activation(B_hi[:], pB_f[:], ACT.Copy).then_inc(hi_done, 1)
            for b in range(KC):
                fold_z_hi(b)
            fold_u_hi(0)
            fold_z_hi(KC)
            fold_u_hi(1)
            exp_margin(1)
            exp_margin(2)
            gated_hi(0)
            u_high(0)
            square_z(0)
            square_z(1)
            square_z(2)
            square_m(0)
            square_z(3)
            square_m(1)
            gated_hi(1)
            square_m(2)
            square_z(4)
            square_m(3)
            u_high(1)
            for t in range(5, NT):
                square_z(t)
                square_m(t - 1)
            square_m(NT - 1)

        @block.vector
        def _(dve):
            steps = {"gate": 0, "gamma": 0}

            def step(kind, instruction):
                s = gate_step if kind == "gate" else gamma_step
                steps[kind] += 1
                instruction.then_inc(s, 1)
                dve.wait_ge(s, steps[kind])

            def split_lo(key, raw, hi, lo):
                dve.wait_ge(hi_done, split_no(*key))
                dve.tensor_tensor(lo, raw, hi.bitcast(F32), ALU.subtract).then_inc(lo_done, 1)

            def language_bias():
                dve.wait_ge(lang_in, 16)
                dve.wait_ge(experts_done, 1)
                ids = lang_i[:].unsqueeze(2).broadcast_to([P, NT, E])
                nums = experts[:].unsqueeze(1).broadcast_to([P, NT, E])
                step("gate", dve.tensor_tensor(chosen[:, :, 0, :], ids, nums, ALU.is_equal))
                step("gate", dve.tensor_scalar(lang_bias[:], chosen[:, :, 0, :], LANG_BIAS, None, ALU.mult))

            def gate_group(g):
                tiles = GROUPS[g]
                t0, t1, n = tiles[0], tiles[-1] + 1, len(tiles)
                hl = bank[GROUP_BANK[g]][:, 0:n * HL].rearrange("p (t c) -> p t c", c=HL)
                dve.wait_ge(hl_done, g + 1)
                step("gate", dve.tensor_tensor(logits[:, t0:t1, :], hl[:, :, ER:HL], lang_bias[:, t0:t1, :], ALU.add))
                for t in tiles:
                    i = dve.max(top8[:, t, :], logits[:, t, :])
                step("gate", i)
                for t in tiles:
                    i = dve.max_index(top8_at[:, t, :], top8[:, t, :], logits[:, t, :])
                dve.tensor_tensor(margin[:, t0:t1], top8[:, t0:t1, 1], top8[:, t0:t1, 0],
                                  ALU.subtract).then_inc(margin_done, 1)
                step("gate", i)
                step("gate", dve.tensor_copy(top_at[:, t0:t1, :], top8_at[:, t0:t1, 0:2]))
                nums = experts[:].unsqueeze(1).unsqueeze(1).broadcast_to([P, n, 2, E])
                at = top_at[:, t0:t1, :].unsqueeze(3).broadcast_to([P, n, 2, E])
                dve.tensor_tensor(chosen[:, t0:t1], nums, at, ALU.is_equal).then_inc(gate_step, 1)
                steps["gate"] += 1
                dve.wait_ge(exp_done, g + 1)
                step("gate", dve.tensor_scalar(half_den[:, t0:t1], e_margin[:, t0:t1], 1.0, 1.0 / SCALING,
                                               ALU.add, ALU.mult))
                step("gate", dve.reciprocal(weight[:, t0:t1, 0], half_den[:, t0:t1]))
                step("gate", dve.tensor_tensor(weight[:, t0:t1, 1], e_margin[:, t0:t1], weight[:, t0:t1, 0], ALU.mult))
                wb = weight[:, t0:t1, :].unsqueeze(3).broadcast_to([P, n, 2, E])
                step("gate", dve.tensor_tensor(chosen_w[:, t0:t1], chosen[:, t0:t1], wb, ALU.mult))
                step("gate", dve.tensor_tensor(gates[:, t0:t1, :], chosen_w[:, t0:t1, 0, :], chosen_w[:, t0:t1, 1, :],
                                               ALU.add))
                for t in tiles:
                    h = hl_at(t)[:, 0:ER].rearrange("p (e r) -> p e r", e=E)
                    dve.tensor_tensor(gated[:, t, :].rearrange("p (e r) -> p e r", e=E), h,
                                      gates[:, t, :].unsqueeze(2).broadcast_to([P, E, R]),
                                      ALU.mult).then_inc(gated_done, 1)

            def fold_z_lo(b):
                dve.wait_ge(mz_hi_done, b + 1)
                dve.tensor_tensor(mz_lo[:, b, :], bank[b][:], mz_hi[:, b, :].bitcast(F32),
                                  ALU.subtract).then_inc(mz_lo_done, 1)

            def fold_u_lo(n):
                dve.wait_ge(mu_hi_done, n + 1)
                if n == 0:
                    dst, hi = mu_lo[:, 0:KC, :], mu_hi[:, 0:KC, :]
                    src = bank[U_FOLD_BANKS[0]][:].rearrange("p (b c) -> p b c", b=KC)
                else:
                    dst, hi = mu_lo[:, KC, :], mu_hi[:, KC, :]
                    src = bank[U_FOLD_BANKS[1]][:, 0:ER]
                dve.tensor_tensor(dst, src, hi.bitcast(F32), ALU.subtract).then_inc(mu_lo_done, 1)

            def gated_lo(h):
                dve.wait_ge(gt_hi_done, h + 1)
                dve.tensor_tensor(gt_lo[:, h, :], bank[GT_BANK[h]][:], gt_hi[:, h, :].bitcast(F32),
                                  ALU.subtract).then_inc(gt_lo_done, 1)

            def u_low(h):
                dve.wait_ge(u_hi_done, h + 1)
                dve.tensor_tensor(u_lo[:, h, :], bank[U_BANK[h]][:], u_hi[:, h, :].bitcast(F32),
                                  ALU.subtract).then_inc(u_lo_done, 1)

            def add_bias(t):
                dve.wait_ge(z_done, t + 1)
                if t == 0:
                    dve.wait_ge(bias_in, 16)
                if t >= 3:
                    dve.wait_ge(z_squared, t - 2)
                    dve.wait_ge(xz_done, t - 2)
                dve.tensor_tensor(z_b[:, t % 3, :], bank[Z_BANKS[t % 3]][:], bias_b[:], ALU.add).then_inc(zb_done, 1)

            def finish(t):
                dve.wait_ge(norm_done, t + 1)
                step("gamma", dve.tensor_scalar(m_den[:, t:t + 1], norm[:, t, 1:2], EPS, 1.0 / C_CLAMP,
                                                ALU.add, ALU.mult))
                step("gamma", dve.reciprocal(m_inv[:, t:t + 1], m_den[:, t:t + 1]))
                step("gamma", dve.tensor_scalar(gamma[:, t:t + 1], norm[:, t, 0:1], m_inv[:, t:t + 1], 1.0,
                                                ALU.mult, ALU.min))
                dve.wait_ge(xz_done, t + 1)
                dve.scalar_tensor_tensor(out=x_out[:, t, :], in0=bank[M_BANKS[t % 2]][:], scalar=gamma[:, t:t + 1],
                                         in1=x_out[:, t, :], op0=ALU.mult, op1=ALU.add).then_inc(out_done, 1)

            split_lo(("fold", 0), fold_f[:, 0, :], fold_hi[:, 0, :], fold_lo[:, 0, :])
            split_lo(("fold", 1), fold_f[:, 1, :], fold_hi[:, 1, :], fold_lo[:, 1, :])
            split_lo(("route", 0), route_f[:], route_hi[:], route_lo[:])
            split_lo(("x", 0), x_f[:, 0], x_hi[:, 0], x_lo[:, 0])
            language_bias()
            split_lo(("fold", 2), fold_f[:, 2, :], fold_hi[:, 2, :], fold_lo[:, 2, :])
            split_lo(("fold", 3), fold_f[:, 3, :], fold_hi[:, 3, :], fold_lo[:, 3, :])
            gate_group(0)
            split_lo(("x", 1), x_f[:, 1], x_hi[:, 1], x_lo[:, 1])
            split_lo(("B", 0), pB_f[:], B_hi[:], B_lo[:])
            for b in range(KC):
                fold_z_lo(b)
            fold_u_lo(0)
            fold_z_lo(KC)
            fold_u_lo(1)
            gate_group(1)
            gate_group(2)
            gated_lo(0)
            u_low(0)
            add_bias(0)
            add_bias(1)
            add_bias(2)
            finish(0)
            add_bias(3)
            finish(1)
            gated_lo(1)
            finish(2)
            add_bias(4)
            finish(3)
            u_low(1)
            for t in range(5, NT):
                add_bias(t)
                finish(t - 1)
            finish(NT - 1)

        @block.tensor
        def _(pe):
            PARTS = ((0, 0), (0, 1), (1, 0))
            fold = (fold_hi, fold_lo)
            route = (route_hi, route_lo)
            x_T = (x_hi, x_lo)
            mz = (mz_hi, mz_lo)
            mu = (mu_hi, mu_lo)
            gt = (gt_hi, gt_lo)
            u_T = (u_hi, u_lo)
            pB = (B_hi, B_lo)

            def fold_chunk(k):
                for b in range(FC):
                    rows = slice(b * P, (b + 1) * P)
                    u_bank = bank[U_FOLD_BANKS[b // KC]]
                    u_cols = slice(b % KC * ER, (b % KC + 1) * ER)
                    for n, (i, j) in enumerate(PARTS):
                        if b == 0 and n == 0:
                            pe.wait_ge(hi_done, split_no("fold", k))
                        if b == 0 and n == 1:
                            pe.wait_ge(lo_done, split_no("fold", k))
                        first, last = k == 0 and n == 0, k == KC - 1 and n == len(PARTS) - 1
                        mm = pe.matmul(bank[b][:], fold[i][:, k, rows], fold[j][:, k, W:W + O],
                                       start=first, stop=last)
                        if last:
                            mm.then_inc(fold_z, 1)
                        mm = pe.matmul(u_bank[:, u_cols], fold[i][:, k, rows], fold[j][:, k, W + O:2 * W],
                                       start=first and b % KC == 0, stop=last, skip_group_check=True)
                        if last and b >= KC - 1:
                            mm.then_inc(fold_u, 1)

            def h_and_logits(g):
                for t in GROUPS[g]:
                    half, cols = t // HT, slice(t % HT * P, (t % HT + 1) * P)
                    pe.wait_ge(lo_done, split_no("x", half))
                    if t == GROUPS[g][0] and GROUP_BANK[g] < FC:
                        pe.wait_ge(mz_lo_done, GROUP_BANK[g] + 1)
                    for k in range(KC):
                        for n, (i, j) in enumerate(PARTS):
                            mm = pe.matmul(hl_at(t), x_T[i][:, half, k, cols], route[j][:, k, :],
                                           start=(k == 0 and n == 0), stop=(k == KC - 1 and n == len(PARTS) - 1),
                                           skip_group_check=True)
                mm.then_inc(hl_done, 1)

            def transpose_gated(half):
                for t in range(half * HT, (half + 1) * HT):
                    pe.wait_ge(gated_done, t + 1)
                    if t == half * HT:
                        g = GROUP_BANK.index(GT_BANK[half])
                        pe.wait_ge(gated_done, GROUPS[g][-1] + 1)
                    mm = pe.transpose(bank[GT_BANK[half]][:, t % HT * P:(t % HT + 1) * P], gated[:, t, :], ident[:])
                mm.then_inc(gt_done, 1)

            def z_of_x(t):
                b = Z_BANKS[t % 3]
                half, cols = t // HT, slice(t % HT * P, (t % HT + 1) * P)
                if t >= 3:
                    pe.wait_ge(zb_done, t - 2)
                for k in range(KC):
                    if t == 0:
                        pe.wait_ge(mz_lo_done, max(b, k) + 1)
                    for n, (i, j) in enumerate(PARTS):
                        if t < 3 and k == 0 and n == 0:
                            pe.wait_ge(mz_lo_done, max(b, k) + 1)
                        pe.matmul(bank[b][:], x_T[i][:, half, k, cols], mz[j][:, k, :],
                                  start=(k == 0 and n == 0), stop=False)

            def z_of_gated(t):
                half, cols = t // HT, slice(t % HT * P, (t % HT + 1) * P)
                pe.wait_ge(gt_lo_done, half + 1)
                pe.wait_ge(mz_lo_done, FC)
                for n, (i, j) in enumerate(PARTS):
                    mm = pe.matmul(bank[Z_BANKS[t % 3]][:], gt[i][:, half, cols], mz[j][:, KC, :],
                                   start=False, stop=(n == len(PARTS) - 1))
                mm.then_inc(z_done, 1)

            def u_of_x(half):
                pe.wait_ge(mu_lo_done, 2)
                if half == 1:
                    pe.wait_ge(gated_done, NT)
                for k in range(KC):
                    for n, (i, j) in enumerate(PARTS):
                        pe.matmul(bank[U_BANK[half]][:], mu[i][:, k, :], x_T[j][:, half, k, :],
                                  start=(k == 0 and n == 0), stop=False)

            def u_of_gated(half):
                pe.wait_ge(gt_lo_done, half + 1)
                for n, (i, j) in enumerate(PARTS):
                    mm = pe.matmul(bank[U_BANK[half]][:], mu[i][:, KC, :], gt[j][:, half, :],
                                   start=False, stop=(n == len(PARTS) - 1))
                mm.then_inc(u_done, 1)

            def m_tile(t):
                half, cols = t // HT, slice(t % HT * P, (t % HT + 1) * P)
                pe.wait_ge(u_lo_done, half + 1)
                if t == 0:
                    pe.wait_ge(lo_done, split_no("B", 0))
                if t >= 2:
                    pe.wait_ge(out_done, t - 1)
                for n, (i, j) in enumerate(PARTS):
                    mm = pe.matmul(bank[M_BANKS[t % 2]][:], u_T[i][:, half, cols], pB[j][:],
                                   start=(n == 0), stop=(n == len(PARTS) - 1))
                mm.then_inc(m_done, 1)

            fold_chunk(0)
            fold_chunk(1)
            h_and_logits(0)
            fold_chunk(2)
            fold_chunk(3)
            h_and_logits(1)
            h_and_logits(2)
            z_of_x(0)
            z_of_x(1)
            u_of_x(0)
            z_of_x(2)
            pe.wait_ge(ident_done, 1)
            transpose_gated(0)
            u_of_gated(0)
            z_of_gated(0)
            z_of_gated(1)
            z_of_gated(2)
            m_tile(0)
            z_of_x(3)
            z_of_gated(3)
            m_tile(1)
            transpose_gated(1)
            m_tile(2)
            z_of_x(4)
            z_of_gated(4)
            m_tile(3)
            u_of_x(1)
            u_of_gated(1)
            for t in range(5, NT):
                z_of_x(t)
                z_of_gated(t)
                m_tile(t - 1)
            m_tile(NT - 1)


def kernel(x, itok_B_0_7, L0_cond_W, L0_cond_Wr, L0_cond_A, L0_cond_B, L0_ffn_W, L0_ffn_b, L0_ffn_A, L0_ffn_B,
           L0_ffn_p_scores):
    import numpy as np
    import concourse.bacc as bacc
    from concourse.bass_utils import run_bass_kernel_spmd

    x, W, Wr, A, B, V, b, C, G, p = (np.asarray(a) for a in (
        x, L0_cond_W, L0_cond_Wr, L0_cond_A, L0_cond_B, L0_ffn_W, L0_ffn_b, L0_ffn_A, L0_ffn_B, L0_ffn_p_scores))
    lang = np.asarray(itok_B_0_7)
    O, D = W.shape
    E, R, _ = A.shape
    T = x.shape[0] * x.shape[1]
    KC, HALF = D // P, T // 2
    x_tok = x.reshape(T, D)
    x_feat = x_tok.reshape(2, HALF, KC, P).transpose(0, 3, 2, 1)
    w_fold = np.concatenate([W, B.transpose(1, 0, 2).reshape(O, E * R), V.T, C.transpose(1, 0, 2).reshape(O, E * R)],
                            axis=1).reshape(KC, P, -1)
    a_route = np.concatenate([A.reshape(E * R, D).T, Wr.T], axis=1).reshape(KC, P, -1).transpose(1, 0, 2)
    arrays = {
        "x_tok": x_tok, "x_feat": x_feat, "w_fold": w_fold, "a_route": a_route,
        "ffn_B": G.reshape(E * R, O), "ffn_b": b, "p_rows": np.repeat(p, R).reshape(P, 1),
        "lang": np.repeat(lang, x.shape[1]).reshape(T // P, P).T,
    }
    arrays = {name: np.ascontiguousarray(a) for name, a in arrays.items()}
    nc = bacc.Bacc("TRN2", target_bir_lowering=False, num_devices=1)
    args = [nc.dram_tensor(name, a.shape, mybir.dt.from_np(a.dtype), kind="ExternalInput").ap()
            for name, a in arrays.items()]
    out = nc.dram_tensor("out", (T, D), mybir.dt.float32, kind="ExternalOutput").ap()
    lora_ffn_kernel(nc, *args, out)
    r = run_bass_kernel_spmd(nc, [arrays], core_ids=[0])
    return r.results[0]["out"].reshape(x.shape)
```

```python
from contextlib import ExitStack

import concourse.bass as bass
import concourse.mybir as mybir

ALU = mybir.AluOpType
ACT = mybir.ActivationFunctionType
AX_X = mybir.AxisListType.X
F32 = mybir.dt.float32
BF16 = mybir.dt.bfloat16
F32R = mybir.dt.float32r
I32 = mybir.dt.int32
U32 = mybir.dt.uint32

P = 128
LANG_BIAS = 5.0
SCALING = 32.0 / 16.0
C_CLAMP = 0.5
EPS = 1e-6


def lora_ffn_kernel(nc: bass.Bass, x_tok, xa_0, x_1, w_fold, ffn_B, ffn_b, p_rows, lang, out):
    T, D = x_tok.shape
    ER, O = ffn_B.shape
    KC = D // P
    FC = KC + 1
    W = D + ER
    NT = T // P
    HT = NT // 2
    HALF = HT * P
    HL = xa_0.shape[2] - HALF
    E = HL - ER
    R = ER // E
    assert D == O == HALF == 512 and ER == P and FC * P == W

    HI, LO = 0, 1
    PRODUCTS = ((HI, HI), (HI, LO), (LO, HI))

    PIECES = [(0, 0, 512, 0, 0), (0, 512, 128, 1, 0), (1, 0, 384, 1, 128), (1, 384, 256, 2, 0),
              (2, 0, 256, 2, 256), (2, 256, 384, 3, 0), (3, 0, 384, 4, 0), (3, 384, 256, 5, 0),
              (4, 0, 256, 5, 256), (4, 256, 384, 6, 0)]
    assert sum(p[2] for p in PIECES) == FC * W
    HL_BANK = (4, 0)
    M_BANKS = (0, 1)
    Z_BANKS = (4, 5, 6)
    GT_BANK = (7, 2)
    U_BANK = (7, 3)

    M_SUM_BANKS = PIECES[-1][3] + 1

    def in_bank(bank):
        return [p for p in PIECES if p[3] == bank]

    def banks_of_block(b):
        return max(p[3] for p in PIECES if p[0] == b) + 1

    SPLITS = ["x0 0 first", "x0 0 rest", "x0 1", "x0 2", "x0 3",
              "out 0", "in 0", "out 1", "in 1", "out 2", "in 2", "out 3", "in 3", "x1", "B"]
    SIDES = {"in": slice(0, W), "out": slice(W, 2 * W)}
    LAST_COLS = (slice(0, O // 2), slice(O // 2, O))
    FIRST, REST = slice(0, HL + P), slice(HL + P, HL + HALF)

    def split_no(name):
        return SPLITS.index(name) + 1

    with ExitStack() as ctx:
        def sb(name, shape, dt):
            return ctx.enter_context(nc.sbuf_tensor(name, shape, dt))

        def sem(name):
            return ctx.enter_context(nc.semaphore(name))

        xa_f = sb("xa_f", [P, KC, HL + HALF], F32)
        x1_f = sb("x1_f", [P, KC, HALF], F32)
        fold_f = sb("fold_f", [P, KC, 2 * W], F32)
        B_f = sb("B_f", [P, O], F32)
        x_out = sb("x_out", [P, NT, D], F32)
        bias_b = sb("bias_b", [P, O], F32)
        p_col = sb("p_col", [P, 1], F32)
        lang_i = sb("lang_i", [P, NT], I32)

        xa = sb("xa", [P, KC, 2, HL + HALF], F32R)
        x1 = sb("x1", [P, 2, KC, HALF], F32R)
        fold = sb("fold", [P, KC, 2, 2 * W], F32R)
        pB_f = sb("pB_f", [P, O], F32)
        pB = sb("pB", [P, 2, O], F32R)
        M = sb("M", [P, FC, 2, W], F32R)
        gt = sb("gt", [P, 2, 2, HALF], F32R)
        u = sb("u", [P, 2, 2, HALF], F32R)

        idle = sb("idle", [P, 512], BF16)

        ident = sb("ident", [P, P], F32)
        experts = sb("experts", [P, E], F32)
        lang_hit = sb("lang_hit", [P, NT, E], F32)
        lang_bias = sb("lang_bias", [P, NT, E], F32)
        hl_part = sb("hl_part", [P, NT, HL], F32)
        hl = sb("hl", [P, NT, HL], F32)
        logits = sb("logits", [P, NT, E], F32)
        top8 = sb("top8", [P, NT, 8], F32)
        top8_at = sb("top8_at", [P, NT, 8], U32)
        top_at = sb("top_at", [P, NT, 2], F32)
        margin = sb("margin", [P, NT], F32)
        e_margin = sb("e_margin", [P, NT], F32)
        half_den = sb("half_den", [P, NT], F32)
        weight = sb("weight", [P, NT, 2], F32)
        chosen = sb("chosen", [P, NT, 2, E], F32)
        chosen_w = sb("chosen_w", [P, NT, 2, E], F32)
        gates = sb("gates", [P, NT, E], F32)
        gated = sb("gated", [P, NT, ER], F32)

        z_b = sb("z_b", [P, 3, O], F32)
        square = fold_f[:, 0:2, 0:O]
        norm2 = sb("norm2", [P, NT, 2], F32)
        norm = sb("norm", [P, NT, 2], F32)
        m_den = sb("m_den", [P, NT], F32)
        m_inv = sb("m_inv", [P, NT], F32)
        gamma = sb("gamma", [P, NT], F32)

        ps = ctx.enter_context(nc.psum_tensor("ps", [P, 8, 512], F32))

        xa_first_in = sem("xa_first_in")
        xa_in = [sem(f"xa_in{k}") for k in range(KC)]
        out0_in = sem("out0_in")
        fold_in = [sem(f"fold_in{k}") for k in range(KC)]
        x1_in = sem("x1_in")
        xt_in = [sem(f"xt_in{h}") for h in range(2)]
        B_in = sem("B_in")
        bias_in = sem("bias_in")
        p_in = sem("p_in")
        lang_in = sem("lang_in")
        hi_done = sem("hi_done")
        lo_done = sem("lo_done")
        pB_done = sem("pB_done")
        idle_zeroed = sem("idle_zeroed")
        zeroed = sem("zeroed")
        ident_done = sem("ident_done")
        experts_done = sem("experts_done")
        M_summed = sem("M_summed")
        M_hi_done = sem("M_hi_done")
        M_lo_done = sem("M_lo_done")
        hl_done = sem("hl_done")
        hl_part_done = sem("hl_part_done")
        hl_summed = sem("hl_summed")
        gate_step = sem("gate_step")
        margin_done = sem("margin_done")
        exp_done = sem("exp_done")
        gated_done = sem("gated_done")
        gt_done = sem("gt_done")
        gt_hi_done = sem("gt_hi_done")
        gt_lo_done = sem("gt_lo_done")
        u_done = sem("u_done")
        u_hi_done = sem("u_hi_done")
        u_lo_done = sem("u_lo_done")
        z_done = sem("z_done")
        m_done = sem("m_done")
        zb_done = sem("zb_done")
        z_squared = sem("z_squared")
        m_squared = sem("m_squared")
        norm_done = sem("norm_done")
        gamma_step = sem("gamma_step")
        xz_done = sem("xz_done")
        out_done = sem("out_done")
        stored = sem("stored")

        block = ctx.enter_context(nc.Block())

        @block.sync
        def _(sp):
            sp.dma_start(xa_f[:, 0, FIRST], xa_0[0][:, FIRST]).then_inc(xa_first_in, 16)
            sp.dma_start(xa_f[:, 0, REST], xa_0[0][:, REST]).then_inc(xa_in[0], 16)
            for k in range(1, KC):
                sp.dma_start(xa_f[:, k, :], xa_0[k]).then_inc(xa_in[k], 16)
            sp.dma_start(fold_f[:, 0, SIDES["out"]], w_fold[0][:, SIDES["out"]]).then_inc(out0_in, 16)
            sp.dma_start(fold_f[:, 0, SIDES["in"]], w_fold[0][:, SIDES["in"]]).then_inc(fold_in[0], 16)
            for k in range(1, KC):
                sp.dma_start(fold_f[:, k, :], w_fold[k]).then_inc(fold_in[k], 16)
            sp.dma_start(x1_f[:], x_1).then_inc(x1_in, 16)
            sp.dma_start(B_f[:], ffn_B).then_inc(B_in, 16)
            sp.dma_start(bias_b[:], ffn_b.partition_broadcast(P)).then_inc(bias_in, 16)
            x_rows = x_tok.rearrange("(t p) d -> p t d", p=P)
            for h in range(2):
                tiles = slice(h * HT, (h + 1) * HT)
                sp.dma_start(x_out[:, tiles, :], x_rows[:, tiles, :]).then_inc(xt_in[h], 16)
            for t in range(NT - 1):
                sp.wait_ge(out_done, t + 1)
                sp.dma_start(out[t * P:(t + 1) * P, :], x_out[:, t, :]).then_inc(stored, 16)
            for n, cols in enumerate(LAST_COLS):
                sp.wait_ge(out_done, NT + n)
                sp.dma_start(out[T - P:T, cols], x_out[:, NT - 1, cols]).then_inc(stored, 16)
            sp.wait_ge(stored, 16 * (NT - 1 + len(LAST_COLS)))

        @block.gpsimd
        def _(pool):
            pool.dma_start(lang_i[:], lang).then_inc(lang_in, 16)
            pool.dma_start(p_col[:], p_rows).then_inc(p_in, 16)
            pool.memset(ident[:], 0.0).then_inc(zeroed, 1)
            pool.iota(experts[:], pattern=[[1, E]], base=0, channel_multiplier=0,
                      allow_small_or_imprecise_dtypes=True).then_inc(experts_done, 1)
            pool.wait_ge(zeroed, 1)
            pool.affine_select(out=ident[:], in_=ident[:], compare_op=ALU.not_equal, fill=1.0, base=0,
                               pattern=[[-1, P]], channel_multiplier=1).then_inc(ident_done, 1)
            for t in range(NT):
                if t % HT == 0:
                    pool.wait_ge(xt_in[t // HT], 16)
                pool.wait_ge(zb_done, t + 1)
                pool.tensor_tensor(x_out[:, t, :], x_out[:, t, :], z_b[:, t % 3, :], ALU.add).then_inc(xz_done, 1)

        @block.scalar
        def _(act):
            def split_hi(hi, raw, landed):
                act.wait_ge(landed, 16)
                act.activation(hi, raw, ACT.Copy).then_inc(hi_done, 1)

            def hl_high_low(half):
                act.wait_ge(hl_done, half + 1)
                act.activation(hl_part[:, half * HT:(half + 1) * HT, :], ps[:, HL_BANK[half]:HL_BANK[half] + HT, HL:2 * HL],
                               ACT.Copy).then_inc(hl_part_done, 1)

            def exp_margin(half):
                act.wait_ge(margin_done, half + 1)
                tiles = slice(half * HT, (half + 1) * HT)
                act.activation(e_margin[:, tiles], margin[:, tiles], ACT.Exp).then_inc(exp_done, 1)

            def M_high(bank):
                act.wait_ge(M_summed, bank + 1)
                for b, c, w, _, at in in_bank(bank):
                    i = act.activation(M[:, b, HI, c:c + w], ps[:, bank, at:at + w], ACT.Copy)
                i.then_inc(M_hi_done, 1)

            def gated_high(half):
                act.wait_ge(gt_done, half + 1)
                act.activation(gt[:, half, HI, :], ps[:, GT_BANK[half], :], ACT.Copy).then_inc(gt_hi_done, 1)

            def u_high(half):
                act.wait_ge(u_done, half + 1)
                act.activation(u[:, half, HI, :], ps[:, U_BANK[half], :], ACT.Copy).then_inc(u_hi_done, 1)

            def square_z(t):
                act.wait_ge(zb_done, t + 1)
                if t >= 1:
                    act.wait_ge(z_squared, t)
                act.activation(square[:, 0, :], z_b[:, t % 3, :], ACT.Square,
                               accum_out=norm2[:, t, 0:1]).then_inc(z_squared, 1)

            def square_m(t):
                act.wait_ge(m_done, t + 1)
                if t >= 1:
                    act.wait_ge(m_squared, t)
                act.activation(square[:, 1, :], ps[:, M_BANKS[t % 2], :], ACT.Square,
                               accum_out=norm2[:, t, 1:2]).then_inc(m_squared, 1)
                act.wait_ge(z_squared, t + 1)
                act.wait_ge(m_squared, t + 1)
                act.activation(norm[:, t, :], norm2[:, t, :], ACT.Sqrt).then_inc(norm_done, 1)

            split_hi(xa[:, 0, HI, FIRST], xa_f[:, 0, FIRST], xa_first_in)
            split_hi(xa[:, 0, HI, REST], xa_f[:, 0, REST], xa_in[0])
            for k in range(1, KC):
                split_hi(xa[:, k, HI, :], xa_f[:, k, :], xa_in[k])
            for k in range(KC):
                for side in ("out", "in"):
                    cols = SIDES[side]
                    split_hi(fold[:, k, HI, cols], fold_f[:, k, cols], out0_in if (side, k) == ("out", 0) else fold_in[k])
                if k == 0:
                    hl_high_low(0)
            exp_margin(0)
            split_hi(x1[:, HI], x1_f[:], x1_in)
            act.wait_ge(p_in, 16)
            act.wait_ge(B_in, 16)
            act.activation(pB_f[:], B_f[:], ACT.Copy, scale=p_col[:, 0:1]).then_inc(pB_done, 1)
            act.wait_ge(pB_done, 1)
            act.activation(pB[:, HI, :], pB_f[:], ACT.Copy).then_inc(hi_done, 1)
            gated_high(0)
            for bank in range(M_SUM_BANKS):
                M_high(bank)
            hl_high_low(1)
            exp_margin(1)
            square_z(0)
            u_high(0)
            square_z(1)
            square_m(0)
            square_z(2)
            square_m(1)
            gated_high(1)
            square_z(3)
            square_m(2)
            square_z(4)
            square_m(3)
            u_high(1)
            square_z(5)
            square_m(4)
            square_m(5)
            square_z(6)
            square_m(6)
            square_m(7)

        @block.vector
        def _(dve):
            steps = {gate_step: 0, gamma_step: 0}

            def step(s, instruction):
                steps[s] += 1
                instruction.then_inc(s, 1)
                dve.wait_ge(s, steps[s])

            def split_lo(name, lo, raw, hi):
                dve.wait_ge(hi_done, split_no(name))
                dve.tensor_tensor(lo, raw, hi.bitcast(F32), ALU.subtract).then_inc(lo_done, 1)

            def language_bias():
                dve.wait_ge(lang_in, 16)
                dve.wait_ge(experts_done, 1)
                ids = lang_i[:].unsqueeze(2).broadcast_to([P, NT, E])
                nums = experts[:].unsqueeze(1).broadcast_to([P, NT, E])
                step(gate_step, dve.tensor_tensor(lang_hit[:], ids, nums, ALU.is_equal))
                step(gate_step, dve.tensor_scalar(lang_bias[:], lang_hit[:], LANG_BIAS, None, ALU.mult))

            def hl_sum(half):
                tiles = slice(half * HT, (half + 1) * HT)
                dve.wait_ge(hl_part_done, half + 1)
                dve.tensor_tensor(hl[:, tiles, :], ps[:, HL_BANK[half]:HL_BANK[half] + HT, 0:HL], hl_part[:, tiles, :],
                                  ALU.add).then_inc(hl_summed, 1)

            def gate_half(half):
                tiles = slice(half * HT, (half + 1) * HT)
                dve.wait_ge(hl_summed, half + 1)
                step(gate_step, dve.tensor_tensor(logits[:, tiles, :], hl[:, tiles, ER:HL], lang_bias[:, tiles, :],
                                                  ALU.add))
                for t in range(half * HT, (half + 1) * HT):
                    i = dve.max(top8[:, t, :], logits[:, t, :])
                step(gate_step, i)
                dve.tensor_tensor(margin[:, tiles], top8[:, tiles, 1], top8[:, tiles, 0],
                                  ALU.subtract).then_inc(margin_done, 1)
                for t in range(half * HT, (half + 1) * HT):
                    i = dve.max_index(top8_at[:, t, :], top8[:, t, :], logits[:, t, :])
                step(gate_step, i)
                step(gate_step, dve.tensor_copy(top_at[:, tiles, :], top8_at[:, tiles, 0:2]))
                nums = experts[:].unsqueeze(1).unsqueeze(1).broadcast_to([P, HT, 2, E])
                at = top_at[:, tiles, :].unsqueeze(3).broadcast_to([P, HT, 2, E])
                step(gate_step, dve.tensor_tensor(chosen[:, tiles], nums, at, ALU.is_equal))
                dve.wait_ge(exp_done, half + 1)
                step(gate_step, dve.tensor_scalar(half_den[:, tiles], e_margin[:, tiles], 1.0, 1.0 / SCALING,
                                                  ALU.add, ALU.mult))
                step(gate_step, dve.reciprocal(weight[:, tiles, 0], half_den[:, tiles]))
                step(gate_step, dve.tensor_tensor(weight[:, tiles, 1], e_margin[:, tiles], weight[:, tiles, 0],
                                                  ALU.mult))
                wb = weight[:, tiles, :].unsqueeze(3).broadcast_to([P, HT, 2, E])
                step(gate_step, dve.tensor_tensor(chosen_w[:, tiles], chosen[:, tiles], wb, ALU.mult))
                step(gate_step, dve.tensor_tensor(gates[:, tiles, :], chosen_w[:, tiles, 0, :],
                                                  chosen_w[:, tiles, 1, :], ALU.add))
                dve.tensor_tensor(gated[:, tiles, :].rearrange("p t (e r) -> p t e r", e=E),
                                  hl[:, tiles, 0:ER].rearrange("p t (e r) -> p t e r", e=E),
                                  gates[:, tiles, :].unsqueeze(3).broadcast_to([P, HT, E, R]),
                                  ALU.mult).then_inc(gated_done, 1)

            def M_low(bank):
                dve.wait_ge(M_hi_done, bank + 1)
                for b, c, w, _, at in in_bank(bank):
                    i = dve.tensor_tensor(M[:, b, LO, c:c + w], ps[:, bank, at:at + w],
                                          M[:, b, HI, c:c + w].bitcast(F32), ALU.subtract)
                i.then_inc(M_lo_done, 1)

            def gated_low(half):
                dve.wait_ge(gt_hi_done, half + 1)
                dve.tensor_tensor(gt[:, half, LO, :], ps[:, GT_BANK[half], :], gt[:, half, HI, :].bitcast(F32),
                                  ALU.subtract).then_inc(gt_lo_done, 1)

            def u_low(half):
                dve.wait_ge(u_hi_done, half + 1)
                dve.tensor_tensor(u[:, half, LO, :], ps[:, U_BANK[half], :], u[:, half, HI, :].bitcast(F32),
                                  ALU.subtract).then_inc(u_lo_done, 1)

            def add_bias(t):
                dve.wait_ge(z_done, t + 1)
                if t == 0:
                    dve.wait_ge(bias_in, 16)
                if t >= 3:
                    dve.wait_ge(z_squared, t - 2)
                    dve.wait_ge(xz_done, t - 2)
                dve.tensor_tensor(z_b[:, t % 3, :], ps[:, Z_BANKS[t % 3], :], bias_b[:], ALU.add).then_inc(zb_done, 1)

            def finish(t):
                dve.wait_ge(norm_done, t + 1)
                step(gamma_step, dve.tensor_scalar(m_den[:, t:t + 1], norm[:, t, 1:2], EPS, 1.0 / C_CLAMP,
                                                   ALU.add, ALU.mult))
                step(gamma_step, dve.reciprocal(m_inv[:, t:t + 1], m_den[:, t:t + 1]))
                step(gamma_step, dve.tensor_scalar(gamma[:, t:t + 1], norm[:, t, 0:1], m_inv[:, t:t + 1], 1.0,
                                                   ALU.mult, ALU.min))
                dve.wait_ge(xz_done, t + 1)
                for cols in LAST_COLS if t == NT - 1 else (slice(0, O),):
                    dve.scalar_tensor_tensor(out=x_out[:, t, cols], in0=ps[:, M_BANKS[t % 2], cols],
                                             scalar=gamma[:, t:t + 1], in1=x_out[:, t, cols],
                                             op0=ALU.mult, op1=ALU.add).then_inc(out_done, 1)

            dve.memset(idle[:], 0.0).then_inc(idle_zeroed, 1)
            split_lo("x0 0 first", xa[:, 0, LO, FIRST], xa_f[:, 0, FIRST], xa[:, 0, HI, FIRST])
            split_lo("x0 0 rest", xa[:, 0, LO, REST], xa_f[:, 0, REST], xa[:, 0, HI, REST])
            for k in range(1, KC):
                split_lo(f"x0 {k}", xa[:, k, LO, :], xa_f[:, k, :], xa[:, k, HI, :])
            for k in range(KC):
                for side in ("out", "in"):
                    cols = SIDES[side]
                    split_lo(f"{side} {k}", fold[:, k, LO, cols], fold_f[:, k, cols], fold[:, k, HI, cols])
                if k == 0:
                    hl_sum(0)
            language_bias()
            gate_half(0)
            split_lo("x1", x1[:, LO], x1_f[:], x1[:, HI])
            split_lo("B", pB[:, LO, :], pB_f[:], pB[:, HI, :])
            gated_low(0)
            for bank in range(M_SUM_BANKS):
                M_low(bank)
            hl_sum(1)
            gate_half(1)
            add_bias(0)
            u_low(0)
            add_bias(1)
            finish(0)
            add_bias(2)
            finish(1)
            gated_low(1)
            add_bias(3)
            finish(2)
            add_bias(4)
            finish(3)
            u_low(1)
            add_bias(5)
            finish(4)
            finish(5)
            add_bias(6)
            finish(6)
            add_bias(7)
            dve.wait_ge(zb_done, NT)
            dve.tensor_tensor_reduce(out=square[:, 0, :], in0=z_b[:, (NT - 1) % 3, :], in1=z_b[:, (NT - 1) % 3, :],
                                     scale=1.0, scalar=0.0, op0=ALU.mult, op1=ALU.add,
                                     accum_out=norm2[:, NT - 1, 0:1]).then_inc(z_squared, 1)
            finish(7)

        @block.tensor
        def _(pe):
            def x_part(half, part, k, cols):
                return xa[:, k, part, HL + cols.start:HL + cols.stop] if half == 0 else x1[:, part, k, cols]

            def tile_cols(t):
                return slice(t % HT * P, (t % HT + 1) * P)

            def h_and_logits(half, k, t):
                bank = HL_BANK[half] + t % HT
                pe.matmul(ps[:, bank, 0:2 * HL].rearrange("p (s c) -> p s c", s=2),
                          x_part(half, HI, k, tile_cols(t)), xa[:, k, :, 0:HL],
                          start=(k == 0), stop=False, skip_group_check=True)
                return pe.matmul(ps[:, bank, 0:HL], x_part(half, LO, k, tile_cols(t)),
                                 xa[:, k, HI, 0:HL],
                                 start=False, stop=(k == KC - 1), skip_group_check=True)

            def fold_product(k, n, i, j):
                b, c, w, bank, at = PIECES[n]
                first, last = k == 0 and (i, j) == PRODUCTS[0], k == KC - 1 and (i, j) == PRODUCTS[-1]
                if first and bank >= HL_BANK[0]:
                    pe.wait_ge(hl_summed, 1)
                mm = pe.matmul(ps[:, bank, at:at + w], fold[:, k, i, b * P:(b + 1) * P],
                               fold[:, k, j, W + c:W + c + w], start=first and at == 0, stop=last,
                               skip_group_check=True)
                if last and PIECES[n] == in_bank(bank)[-1]:
                    mm.then_inc(M_summed, 1)

            def fold_chunk(k):
                pe.wait_ge(hi_done, split_no(f"in {k}"))
                fold_product(k, 0, HI, HI)
                pe.wait_ge(lo_done, split_no(f"out {k}"))
                fold_product(k, 0, HI, LO)
                fold_product(k, 1, HI, HI)
                fold_product(k, 1, HI, LO)
                pe.wait_ge(lo_done, split_no(f"in {k}"))
                fold_product(k, 0, LO, HI)
                fold_product(k, 1, LO, HI)
                for n in range(2, len(PIECES)):
                    for i, j in PRODUCTS:
                        fold_product(k, n, i, j)

            def transpose_gated(half):
                pe.wait_ge(gated_done, half + 1)
                for t in range(half * HT, (half + 1) * HT):
                    mm = pe.transpose(ps[:, GT_BANK[half], tile_cols(t)], gated[:, t, :], ident[:])
                mm.then_inc(gt_done, 1)

            def z_tile(t):
                bank, half = Z_BANKS[t % 3], t // HT
                if t >= 3:
                    pe.wait_ge(zb_done, t - 2)
                else:
                    pe.wait_ge(M_lo_done, bank + 1)
                for k in range(FC):
                    if t == 0:
                        pe.wait_ge(M_lo_done, banks_of_block(k))
                    if k == KC:
                        pe.wait_ge(gt_lo_done, half + 1)
                    for i, j in PRODUCTS:
                        lhs = x_part(half, i, k, tile_cols(t)) if k < KC else gt[:, half, i, tile_cols(t)]
                        mm = pe.matmul(ps[:, bank, :], lhs, M[:, k, j, 0:O],
                                       start=(k == 0 and (i, j) == PRODUCTS[0]),
                                       stop=(k == KC and (i, j) == PRODUCTS[-1]))
                mm.then_inc(z_done, 1)

            def u_half(half):
                for k in range(FC):
                    if k == (0 if half == 0 else KC):
                        pe.wait_ge(gt_lo_done, half + 1)
                    for i, j in PRODUCTS:
                        rhs = x_part(half, j, k, slice(0, HALF)) if k < KC else gt[:, half, j, :]
                        mm = pe.matmul(ps[:, U_BANK[half], :], M[:, k, i, O:W], rhs,
                                       start=(k == 0 and (i, j) == PRODUCTS[0]),
                                       stop=(k == KC and (i, j) == PRODUCTS[-1]))
                mm.then_inc(u_done, 1)

            def m_tile(t):
                half = t // HT
                if t % HT == 0:
                    pe.wait_ge(u_lo_done, half + 1)
                if t == 0:
                    pe.wait_ge(lo_done, split_no("B"))
                    pe.wait_ge(hl_summed, 2)
                if t >= 2:
                    pe.wait_ge(out_done, t - 1)
                for i, j in PRODUCTS:
                    mm = pe.matmul(ps[:, M_BANKS[t % 2], :], u[:, half, i, tile_cols(t)], pB[:, j, :],
                                   start=((i, j) == PRODUCTS[0]), stop=((i, j) == PRODUCTS[-1]))
                mm.then_inc(m_done, 1)

            def keep_busy(times):
                for _ in range(times):
                    pe.matmul(ps[:, 0, :], idle[:, 0:P], idle[:], start=True, stop=True)

            pe.wait_ge(idle_zeroed, 1)
            keep_busy(7)
            for k in range(KC):
                pe.wait_ge(lo_done, split_no(f"x0 {k}" if k else "x0 0 first"))
                for t in range(HT):
                    if (k, t) == (0, 1):
                        keep_busy(1)
                        pe.wait_ge(lo_done, split_no("x0 0 rest"))
                    mm = h_and_logits(0, k, t)
            mm.then_inc(hl_done, 1)
            fold_chunk(0)
            fold_chunk(1)
            fold_chunk(2)
            pe.wait_ge(ident_done, 1)
            transpose_gated(0)
            fold_chunk(3)
            pe.wait_ge(lo_done, split_no("x1"))
            for t in range(HT, NT):
                pe.wait_ge(M_lo_done, HL_BANK[1] + t % HT + 1)
                for k in range(KC):
                    mm = h_and_logits(1, k, t)
            mm.then_inc(hl_done, 1)
            z_tile(0)
            u_half(0)
            z_tile(1)
            m_tile(0)
            z_tile(2)
            m_tile(1)
            transpose_gated(1)
            z_tile(3)
            m_tile(2)
            z_tile(4)
            m_tile(3)
            u_half(1)
            z_tile(5)
            m_tile(4)
            m_tile(5)
            z_tile(6)
            m_tile(6)
            z_tile(7)
            m_tile(7)


def kernel(x, itok_B_0_7, L0_cond_W, L0_cond_Wr, L0_cond_A, L0_cond_B, L0_ffn_W, L0_ffn_b, L0_ffn_A, L0_ffn_B,
           L0_ffn_p_scores):
    import numpy as np
    import concourse.bacc as bacc
    from concourse.bass_utils import run_bass_kernel_spmd

    x, W, Wr, A, B, V, b, C, G, p = (np.asarray(a) for a in (
        x, L0_cond_W, L0_cond_Wr, L0_cond_A, L0_cond_B, L0_ffn_W, L0_ffn_b, L0_ffn_A, L0_ffn_B, L0_ffn_p_scores))
    lang = np.asarray(itok_B_0_7)
    O, D = W.shape
    E, R, _ = A.shape
    T = x.shape[0] * x.shape[1]
    KC, HALF = D // P, T // 2
    x_tok = x.reshape(T, D)
    x_feat = x_tok.reshape(2, HALF, KC, P).transpose(0, 2, 3, 1)
    w_fold = np.concatenate([W, B.transpose(1, 0, 2).reshape(O, E * R), V.T, C.transpose(1, 0, 2).reshape(O, E * R)],
                            axis=1).reshape(KC, P, -1)
    a_route = np.concatenate([A.reshape(E * R, D).T, Wr.T], axis=1).reshape(KC, P, -1)
    xa_0 = np.concatenate([a_route, x_feat[0]], axis=2)
    arrays = {
        "x_tok": x_tok, "xa_0": xa_0, "x_1": x_feat[1].transpose(1, 0, 2), "w_fold": w_fold,
        "ffn_B": G.reshape(E * R, O), "ffn_b": b, "p_rows": np.repeat(p, R).reshape(P, 1),
        "lang": np.repeat(lang, x.shape[1]).reshape(T // P, P).T,
    }
    arrays = {name: np.ascontiguousarray(a) for name, a in arrays.items()}
    nc = bacc.Bacc("TRN2", target_bir_lowering=False, num_devices=1)
    args = [nc.dram_tensor(name, a.shape, mybir.dt.from_np(a.dtype), kind="ExternalInput").ap()
            for name, a in arrays.items()]
    out = nc.dram_tensor("out", (T, D), mybir.dt.float32, kind="ExternalOutput").ap()
    lora_ffn_kernel(nc, *args, out)
    r = run_bass_kernel_spmd(nc, [arrays], core_ids=[0])
    return r.results[0]["out"].reshape(x.shape)
```
